# Optimizing a Trainium2 kernel written in Bass

```python
import numpy as np
import jax
import jax.numpy as jnp

def _softmax(x, axis=-1):
    return jax.nn.softmax(x, axis=axis)

def _gelu(x):
    return jax.nn.gelu(x, approximate=True)

def _silu(x):
    return jax.nn.silu(x)

def _sigmoid(x):
    return jax.nn.sigmoid(x)

def _layernorm(x, axis=-1, eps=1e-05):
    m = jnp.mean(x, axis=axis, keepdims=True)
    v = jnp.var(x, axis=axis, keepdims=True)
    return (x - m) / jnp.sqrt(v + eps)

def _scatter_add(tgt, idx, src, axis=0):
    return tgt.at[idx].add(src)

def _segment_sum(src, seg, n):
    return jax.ops.segment_sum(src, seg, n)
kernel_name = 'mk_adj_ffn_d1_adj_r2_981457'

def setup_inputs(seed: int=0):
    np.random.seed(seed)
    _w = jnp.asarray

    def _rec_inputs():
        import jax
        import jax.numpy as jnp
        _gk = jax.random.key(seed)
        x = -0.0003929 + 0.9999 * jax.random.normal(jax.random.fold_in(_gk, 1), (16, 512, 128), jnp.float32)
        _a = jax.random.bernoulli(jax.random.fold_in(_gk, 2), 0.0078125, (512, 512))
        _a = jnp.logical_or(_a, jnp.swapaxes(_a, -1, -2))
        _a = jnp.logical_or(_a, jnp.eye(512, dtype=bool))
        _af = _a.astype(jnp.float32)
        _af = _af * jax.random.uniform(jax.random.fold_in(_gk, 3), (512, 512), jnp.float32, 0.05, 1)
        adj = _af
        return (x, adj)
    x, adj = _rec_inputs()

    def _L0_gnn_setup():
        import jax, jax.numpy as jnp
        import numpy as np
        EPS = 1e-05

        def _batchnorm(x, gamma, beta):
            mu = jnp.mean(x, axis=0)
            var = jnp.var(x, axis=0)
            return (x - mu) * jax.lax.rsqrt(var + EPS) * gamma + beta
        key = jax.random.key(seed)
        ks = jax.random.split(key, 4)
        b, n, d, h, o = (32, 1024, 128, 256, 128)
        features = jax.random.normal(ks[0], (b, n, d), dtype=jnp.float32)
        A = jax.random.uniform(ks[1], (n, n), dtype=jnp.float32)
        lim1 = float(np.sqrt(6.0 / (d + h)))
        W1 = jax.random.uniform(ks[2], (h, d), minval=-lim1, maxval=lim1, dtype=jnp.float32)
        b1 = jnp.zeros((h,), jnp.float32)
        lim2 = float(np.sqrt(6.0 / (h + o)))
        W2 = jax.random.uniform(ks[3], (o, h), minval=-lim2, maxval=lim2, dtype=jnp.float32)
        b2 = jnp.zeros((o,), jnp.float32)
        g1 = jnp.ones((h,), jnp.float32)
        be1 = jnp.zeros((h,), jnp.float32)
        g2 = jnp.ones((o,), jnp.float32)
        be2 = jnp.zeros((o,), jnp.float32)
        return {'features': features, 'A': A, 'W1': W1, 'b1': b1, 'g1': g1, 'be1': be1, 'W2': W2, 'b2': b2, 'g2': g2, 'be2': be2}
    _L0_gnn_all = _L0_gnn_setup()
    _L0_gnn_in = {k: v for k, v in _L0_gnn_all.items() if k in ('W1', 'b1', 'g1', 'be1', 'W2', 'b2', 'g2', 'be2')}
    del _L0_gnn_all

    def _L0_ffn_setup():
        import jax, jax.numpy as jnp
        import numpy as np
        DIM = 128
        HEADS = 8
        NUM_KEYS = 128
        NUM_KV = NUM_KEYS ** 2
        PK_TOPK = 16
        FINAL_TOPK = 16
        DIM_KEY = DIM // 2
        P = 2

        def _pk(x, Wq_pk, pk_keys):
            b, n, _ = x.shape
            q = (x @ Wq_pk).reshape(b, n, P, HEADS, DIM_KEY).transpose(2, 0, 1, 3, 4)
            sim = jnp.einsum('pbnhd,pkhd->pbnhk', q, pk_keys)
            scores, idx = jax.lax.top_k(sim, PK_TOPK)
            idx0 = idx[0]
            idx1 = idx[1] * NUM_KEYS
            index = (idx0[..., :, None] + idx1[..., None, :]).reshape(b, n, HEADS, PK_TOPK * PK_TOPK)
            score = (scores[0][..., :, None] + scores[1][..., None, :]).reshape(b, n, HEADS, PK_TOPK * PK_TOPK)
            final_scores, pk_idx = jax.lax.top_k(score, FINAL_TOPK)
            final_indices = jnp.take_along_axis(index, pk_idx, axis=-1)
            final_scores = jax.nn.softmax(final_scores, axis=-1)
            return (final_scores, final_indices)
        key = jax.random.key(seed)
        ks = jax.random.split(key, 7)
        b, n = (2, 512)
        std = 0.02
        x = jax.random.normal(ks[0], (b, n, DIM), dtype=jnp.float32)
        Wq_pk = jax.random.normal(ks[1], (DIM, P * HEADS * DIM_KEY), dtype=jnp.float32) * std
        pk_keys = jax.random.normal(ks[2], (P, NUM_KEYS, HEADS, DIM_KEY), dtype=jnp.float32) * std
        Wq = jax.random.normal(ks[3], (DIM, HEADS * DIM), dtype=jnp.float32) * std
        keys_table = jax.random.normal(ks[4], (NUM_KV * HEADS, DIM), dtype=jnp.float32) * std
        values_table = jax.random.normal(ks[5], (NUM_KV * HEADS, DIM), dtype=jnp.float32) * std
        Wo = jax.random.normal(ks[6], (DIM * HEADS, DIM), dtype=jnp.float32) * std
        return {'x': x, 'Wq_pk': Wq_pk, 'pk_keys': pk_keys, 'Wq': Wq, 'keys_table': keys_table, 'values_table': values_table, 'Wo': Wo}
    _L0_ffn_all = _L0_ffn_setup()
    _L0_ffn_in = {k: v for k, v in _L0_ffn_all.items() if k in ('Wq_pk', 'pk_keys', 'Wq', 'keys_table', 'values_table', 'Wo')}
    del _L0_ffn_all
    return {'x': x, 'adj': adj, 'L0_gnn_W1': _L0_gnn_in['W1'], 'L0_gnn_b1': _L0_gnn_in['b1'], 'L0_gnn_g1': _L0_gnn_in['g1'], 'L0_gnn_be1': _L0_gnn_in['be1'], 'L0_gnn_W2': _L0_gnn_in['W2'], 'L0_gnn_b2': _L0_gnn_in['b2'], 'L0_gnn_g2': _L0_gnn_in['g2'], 'L0_gnn_be2': _L0_gnn_in['be2'], 'L0_ffn_Wq_pk': _L0_ffn_in['Wq_pk'], 'L0_ffn_pk_keys': _L0_ffn_in['pk_keys'], 'L0_ffn_Wq': _L0_ffn_in['Wq'], 'L0_ffn_keys_table': _L0_ffn_in['keys_table'], 'L0_ffn_values_table': _L0_ffn_in['values_table'], 'L0_ffn_Wo': _L0_ffn_in['Wo']}

def reference(x, adj, L0_gnn_W1, L0_gnn_b1, L0_gnn_g1, L0_gnn_be1, L0_gnn_W2, L0_gnn_b2, L0_gnn_g2, L0_gnn_be2, L0_ffn_Wq_pk, L0_ffn_pk_keys, L0_ffn_Wq, L0_ffn_keys_table, L0_ffn_values_table, L0_ffn_Wo):
    import jax
    import jax.numpy as jnp

    def _L0_gnn_ref(features, A, W1, b1, g1, be1, W2, b2, g2, be2):
        import jax, jax.numpy as jnp
        import numpy as np
        EPS = 1e-05

        def _batchnorm(x, gamma, beta):
            mu = jnp.mean(x, axis=0)
            var = jnp.var(x, axis=0)
            return (x - mu) * jax.lax.rsqrt(var + EPS) * gamma + beta
        b, n, d = features.shape
        A_norm = A + jnp.eye(n, dtype=A.dtype)
        deg = jnp.sum(A_norm, axis=0) + jnp.sum(A_norm, axis=1) - jnp.diagonal(A_norm)
        dinv = jax.lax.rsqrt(deg)
        A_hat = A_norm * dinv[:, None] * dinv[None, :]
        agg = jnp.einsum('nm,bmd->bnd', A_hat, features)
        x = agg.reshape(-1, d)
        h = jax.nn.relu(_batchnorm(x @ W1.T + b1, g1, be1))
        out = h @ W2.T + b2
        out = _batchnorm(out, g2, be2)
        return out.reshape(b, n, -1)

    def _L0_ffn_ref(x, Wq_pk, pk_keys, Wq, keys_table, values_table, Wo):
        import jax, jax.numpy as jnp
        import numpy as np
        DIM = 128
        HEADS = 8
        NUM_KEYS = 128
        NUM_KV = NUM_KEYS ** 2
        PK_TOPK = 16
        FINAL_TOPK = 16
        DIM_KEY = DIM // 2
        P = 2

        def _pk(x, Wq_pk, pk_keys):
            b, n, _ = x.shape
            q = (x @ Wq_pk).reshape(b, n, P, HEADS, DIM_KEY).transpose(2, 0, 1, 3, 4)
            sim = jnp.einsum('pbnhd,pkhd->pbnhk', q, pk_keys)
            scores, idx = jax.lax.top_k(sim, PK_TOPK)
            idx0 = idx[0]
            idx1 = idx[1] * NUM_KEYS
            index = (idx0[..., :, None] + idx1[..., None, :]).reshape(b, n, HEADS, PK_TOPK * PK_TOPK)
            score = (scores[0][..., :, None] + scores[1][..., None, :]).reshape(b, n, HEADS, PK_TOPK * PK_TOPK)
            final_scores, pk_idx = jax.lax.top_k(score, FINAL_TOPK)
            final_indices = jnp.take_along_axis(index, pk_idx, axis=-1)
            final_scores = jax.nn.softmax(final_scores, axis=-1)
            return (final_scores, final_indices)
        b, n, d = x.shape
        q = (x @ Wq).reshape(b, n, HEADS, DIM) * DIM ** (-0.5)
        kv_scores, indices = _pk(x, Wq_pk, pk_keys)
        offsets = jnp.arange(HEADS, dtype=indices.dtype) * NUM_KV
        ind = indices + offsets[None, None, :, None]
        k = jnp.einsum('bnhk,bnhkd->bnhd', kv_scores, keys_table[ind])
        v = jnp.einsum('bnhk,bnhkd->bnhd', kv_scores, values_table[ind])
        sim = jnp.einsum('bihd,bjhd->bhij', q, k)
        neg = -jnp.finfo(sim.dtype).max
        causal = jnp.tril(jnp.ones((n, n), dtype=bool))
        sim = jnp.where(causal, sim, neg)
        attn = jax.nn.softmax(sim, axis=-1)
        out = jnp.einsum('bhij,bjhd->bhid', attn, v)
        out = out.transpose(0, 2, 1, 3).reshape(b, n, HEADS * DIM)
        return out @ Wo
    x = x + _L0_gnn_ref(_layernorm(x, axis=-1), adj, L0_gnn_W1, L0_gnn_b1, L0_gnn_g1, L0_gnn_be1, L0_gnn_W2, L0_gnn_b2, L0_gnn_g2, L0_gnn_be2)
    x = x + _L0_ffn_ref(_layernorm(x, axis=-1), L0_ffn_Wq_pk, L0_ffn_pk_keys, L0_ffn_Wq, L0_ffn_keys_table, L0_ffn_values_table, L0_ffn_Wo)
    return x

_drawn_inputs = setup_inputs


def setup_inputs(seed=0):
    import zlib

    import numpy as np

    out = dict(_drawn_inputs(seed))
    spreads = {'L0_gnn_b1': (0.0, 2.0),
     'L0_gnn_g1': (1.0, 0.2),
     'L0_gnn_be1': (0.0, 0.1),
     'L0_gnn_b2': (0.0, 2.0),
     'L0_gnn_g2': (1.0, 0.2),
     'L0_gnn_be2': (0.0, 0.1)}
    factors = {'L0_ffn_Wq_pk': 8.0,
     'L0_ffn_pk_keys': 8.0,
     'L0_ffn_Wq': 64.0,
     'L0_ffn_keys_table': 64.0,
     'L0_ffn_values_table': 8.0,
     'L0_ffn_Wo': 8.0}
    for name, (base, spread) in spreads.items():
        noise = np.random.default_rng([zlib.crc32(name.encode()), seed]).standard_normal(out[name].shape)
        drawn = base * np.exp(spread * noise) if base else spread * noise
        out[name] = jnp.asarray(drawn.astype(out[name].dtype))
    for name, factor in factors.items():
        out[name] = (out[name] * factor).astype(out[name].dtype)
    return out
```

```python
import concourse.bass as bass
from concourse import mybir
from contextlib import ExitStack

P = 128
BATCH, SEQ = 16, 512
TILES = SEQ // P
HEADS = 8
NUM_KEYS = 128
TOPK = 16
DIM_KEY = 64
HIDDEN = 256
CHUNKS = HIDDEN // P
EPS = 1e-5
UNITS = TILES * HEADS
RING = 4
DVE_ROWS = 8
PE_ROWS = TOPK - DVE_ROWS
PREP_AHEAD = 4
SCORES_AHEAD = 5
NUM_KV = NUM_KEYS * NUM_KEYS
PAD_TILES = 3
LOWEST = -3.4028234e38
MASKED = -3.0e38

BLOCKS = [(0, 1, 16), (1, 1, 8), (2, 2, 5), (4, 4, 3), (8, 8, 1)]
assert all(any(i0 <= i < i0 + n and j < m for i0, n, m in BLOCKS)
           for i in range(TOPK) for j in range(TOPK) if (i + 1) * (j + 1) <= TOPK)
CANDS = sum(n * m for _, n, m in BLOCKS)

ROW_SHIFT = 16
ROW_BIAS = 128
LOW_BITS = 15


class Chain:

    def __init__(self, eng, sem):
        self.eng, self.sem, self.n = eng, sem, 0

    def add(self, instruction):
        self.n += 1
        instruction.then_inc(self.sem, 1)

    def wait(self):
        self.eng.wait_ge(self.sem, self.n)

    def restart(self):
        self.wait()
        self.eng.sem_clear(self.sem)
        self.n = 0


def build(nc, x, adj, vecs, w1t, w2t, wqpk_t, keys_t, wq, table, wo, out):
    f32, i32, u32 = mybir.dt.float32, mybir.dt.int32, mybir.dt.uint32
    ALU, ACT, AX = mybir.AluOpType, mybir.ActivationFunctionType, mybir.AxisListType

    x_tiles = x.rearrange("(t p) d -> t p d", p=P)
    out_tiles = out.rearrange("b (t p) d -> (b t) p d", p=P)

    with ExitStack() as ctx:
        def sb(name, shape, dt=f32):
            return ctx.enter_context(nc.sbuf_tensor(name, shape, dt))

        def sem(name):
            return ctx.enter_context(nc.semaphore(name))

        big = sb("big", [P, RING * TOPK * 2 * P])
        h1 = big[:, :].rearrange("p (c n) -> p c n", c=CHUNKS)
        rows = big[:, :].rearrange("p (r k n) -> p r k n", r=RING, k=TOPK)
        k_store = sb("k_store", [P, HEADS, SEQ])
        flat = k_store[:, :, :].rearrange("p h n -> p (h n)")
        adj_sb = flat[:, 0:TILES * SEQ].rearrange("p (m n) -> p m n", m=TILES)
        adj_t = flat[:, TILES * SEQ:2 * TILES * SEQ].rearrange("p (m n) -> p m n", m=TILES)
        v_store = sb("v_store", [P, HEADS, TILES, P])
        flat = v_store[:, :, :, :].rearrange("p h t d -> p (h t d)")
        x_batch, x_norm, agg = (flat[:, i * 2 * SEQ:(i + 1) * 2 * SEQ].rearrange("p (j n) -> p j n", j=2)
                                for i in range(3))
        diag_tmp = flat[:, 3 * 2 * SEQ:3 * 2 * SEQ + SEQ].rearrange("p (m n) -> p m n", m=TILES)
        diags = sb("diags", [P, 2, PE_ROWS, P])
        flat = diags[:, :, :, :].rearrange("p j k n -> p (j k n)")
        hid_relu = flat[:, 0:2 * CHUNKS * SEQ].rearrange("p (j c n) -> p j c n", j=2, c=CHUNKS)
        wqpk_sb = flat[0:DIM_KEY, 0:2 * HEADS * P]
        keys_sb = sb("keys_sb", [DIM_KEY, 2 * HEADS * P])
        gnn_out = sb("gnn_out", [P, (BATCH * TILES + 1) * P])

        fold = sb("fold", [P, HEADS, 2, NUM_KEYS])
        wq_sb = sb("wq_sb", [P, HEADS * P])
        wo_sb = sb("wo_sb", [P, HEADS, P])
        w1_sb = sb("w1_sb", [P, HIDDEN])
        w2_sb = sb("w2_sb", [P, CHUNKS, P])
        vec_sb = sb("vec_sb", [P, 9])
        b1, g1, be1 = (vec_sb[:, i * CHUNKS:(i + 1) * CHUNKS] for i in range(3))
        b2, g2, be2 = (vec_sb[:, 6 + i:7 + i] for i in range(3))
        ident = sb("ident", [P, P])
        causal = sb("causal", [P, P])
        ones = sb("ones", [P, 1])
        eps = sb("eps", [P, 1])

        row_sum, diag_sum, degree, root, dinv = (
            sb(n, [P, TILES]) for n in ("row_sum", "diag_sum", "degree", "root", "dinv"))
        x_stats = sb("x_stats", [P, TILES, 6])
        x_mv = sb("x_mv", [P, 2, TILES, 2])
        x_std = sb("x_std", [P, 2, TILES])
        x_rstd = sb("x_rstd", [P, TILES])
        h_stats = sb("h_stats", [P, CHUNKS, BATCH * 6])
        o_stats = sb("o_stats", [P, BATCH * 6])
        h_mv, o_mv = sb("h_mv", [P, CHUNKS, 2]), sb("o_mv", [P, 1, 2])
        h_std, h_scale, h_tmp, h_shift = (sb(n, [P, CHUNKS]) for n in ("h_std", "h_scale", "h_tmp", "h_shift"))
        o_std, o_scale, o_tmp, o_shift = (sb(n, [P, 1]) for n in ("o_std", "o_scale", "o_tmp", "o_shift"))

        x_in = sb("x_in", [P, 2, P])
        y_t = sb("y_t", [P, P])
        x1 = sb("x1", [P, 2, P])
        t_stats, t_mv, t_std, t_rstd = sb("t_stats", [P, 6]), sb("t_mv", [P, 2]), sb("t_std", [P, 1]), sb("t_rstd", [P, 1])
        x2 = sb("x2", [P, P])
        x2_t = sb("x2_t", [P, 2, P])

        scores = sb("scores", [P, 2, 2, NUM_KEYS])
        rest = sb("rest", [P, 2, NUM_KEYS])
        top_i = sb("top_i", [P, 2, TOPK], u32)
        top = sb("top", [P, 2, 2, TOPK])
        cand = sb("cand", [P, 2, CANDS])
        best = sb("best", [P, TOPK])
        neg_best = sb("neg_best", [P, 1])
        left1, left2 = sb("left1", [P, CANDS]), sb("left2", [P, CANDS])
        picked = sb("picked", [P, CANDS], i32)
        sum_exp = sb("sum_exp", [P, CANDS])
        code = sb("code", [P, 2, CANDS], i32)
        code_left = sb("code_left", [P, 2, CANDS])
        got = sb("got", [P, 2, TOPK])
        got_row, got_high = sb("got_row", [P, TOPK], i32), sb("got_high", [P, TOPK], i32)
        row_index = sb("row_index", [P, HEADS, TOPK], u32)
        weight = sb("weight", [P, HEADS, TOPK])
        weight_sum = sb("weight_sum", [P, 1])
        weight_rsum = sb("weight_rsum", [P, HEADS])

        kv_part = sb("kv_part", [P, 2 * P])
        k_now = sb("k_now", [P, P])
        q_t = sb("q_t", [P, 2, P])
        neg_max = sb("neg_max", [P, 2])
        probs = sb("probs", [P, SEQ])
        prob_sum, prob_rsum = sb("prob_sum", [P, 2]), sb("prob_rsum", [P, 1])
        probs_t = sb("probs_t", [P, SEQ])
        att_t = sb("att_t", [P, P])
        result = sb("result", [P, 2, P])

        bank = [ctx.enter_context(nc.psum_tensor(f"bank{i}", [P, SEQ], f32)) for i in range(8)]
        ps_scores, ps_sim, ps_probs_t, ps_att, ps_turn, ps_y = (bank[i] for i in (0, 3, 4, 5, 6, 7))
        ps_kv, ps_part = bank[1], bank[2]

        adj_in, small_in, fold_in, attn_w_in = sem("adj_in"), sem("small_in"), sem("fold_in"), sem("attn_w_in")
        consts_made, mask_made, memsets_made = sem("consts_made"), sem("mask_made"), sem("memsets_made")
        adj_plus_i, col_sums, degree_made, degree_root, dinv_made = (
            sem(n) for n in ("adj_plus_i", "col_sums", "degree_made", "degree_root", "dinv_made"))
        adj_scaled, adj_turned, adj_t_made = sem("adj_scaled"), sem("adj_turned"), sem("adj_t_made")
        fold_mm, fold_made = sem("fold_mm"), sem("fold_made")
        x_batch_in = [sem(f"x_batch_in{j}") for j in range(2)]
        ln_stats, ln_std, x_norm_made = sem("ln_stats"), sem("ln_std"), sem("x_norm_made")
        agg_mm, agg_made, h1_mm, h1_made = sem("agg_mm"), sem("agg_made"), sem("h1_mm"), sem("h1_made")
        bn1_var, bn1_std, bn1_made = sem("bn1_var"), sem("bn1_std"), sem("bn1_made")
        relu_made, out_mm, gnn_out_made = sem("relu_made"), sem("out_mm"), sem("gnn_out_made")
        bn2_var, bn2_std, bn2_made = sem("bn2_var"), sem("bn2_std"), sem("bn2_made")
        x_in_ready = [sem(f"x_in_ready{j}") for j in range(2)]
        y_made, y_turned, x1_stats, x1_std, x2_made, x2_turned, front_done = (
            sem(n) for n in ("y_made", "y_turned", "x1_stats", "x1_std", "x2_made", "x2_turned", "front_done"))
        scores_mm, scores_ready, best_ready, exp_ready = (
            sem(n) for n in ("scores_mm", "scores_ready", "best_ready", "exp_ready"))
        index_ready, weights_ready, diags_ready = sem("index_ready"), sem("weights_ready"), sem("diags_ready")
        part_ready = sem("part_ready")
        rows_in = [sem(f"rows_in{h}") for h in range(HEADS)]
        combined, kv_ready, kq_mm, kq_ready = sem("combined"), sem("kv_ready"), sem("kq_mm"), sem("kq_ready")
        sim_ready, max_ready, probs_exp, probs_ready = (
            sem(n) for n in ("sim_ready", "max_ready", "probs_exp", "probs_ready"))
        probs_turned, probs_t_ready, att_mm, att_ready = (
            sem(n) for n in ("probs_turned", "probs_t_ready", "att_mm", "att_ready"))
        y_done, result_ready, result_stored, out_stored = (
            sem(n) for n in ("y_done", "result_ready", "result_stored", "out_stored"))
        dve_own = sem("dve_own")
        dve_gate, pool_gate = sem("dve_gate"), sem("pool_gate")

        block = ctx.enter_context(nc.Block())

        @block.sync
        def _(sp):
            sp.dma_start(adj_sb, adj.rearrange("(m p) n -> p m n", p=P)).then_inc(adj_in, 16)
            sp.dma_start(vec_sb[:, :], vecs).then_inc(small_in, 16)
            sp.dma_start(w1_sb[:, :], w1t).then_inc(small_in, 16)
            sp.dma_start(w2_sb[:, :, :], w2t).then_inc(small_in, 16)
            with sp.Fori(0, BATCH // 2) as b2_:
                for j in range(2):
                    n = b2_ * 2 + j
                    sp.wait_ge(x_norm_made, n + 1)
                    sp.dma_start(x_batch[:, j, :].rearrange("p (m d) -> p m d", m=TILES),
                                 x_tiles[bass.ds(n * TILES, TILES)].rearrange("m p d -> p m d")
                                 ).then_inc(x_batch_in[j], 16)
            sp.dma_start(wq_sb[:, :], wq).then_inc(attn_w_in, 16)
            sp.dma_start(wo_sb[:, :, :], wo).then_inc(attn_w_in, 16)
            for j in range(2):
                sp.dma_start(x_in[:, j, :], x_tiles[j]).then_inc(x_in_ready[j], 16)
            sp.wait_ge(x1_stats, 1)
            sp.dma_start(x_in[:, 0, :], x_tiles[2]).then_inc(x_in_ready[0], 16)
            with sp.Fori(0, BATCH) as b:
                for ti in range(TILES):
                    t = b * TILES + ti
                    sp.wait_ge(x1_stats, t + 2)
                    j = (ti + 1) % 2
                    sp.dma_start(x_in[:, j, :], x_tiles[bass.ds(t + 3, 1)].rearrange("a p d -> p (a d)")
                                 ).then_inc(x_in_ready[j], 16)
                    sp.wait_ge(result_ready, t + 2)
                    sp.dma_start(out_tiles[bass.ds(t, 1)].rearrange("a p d -> p (a d)"), result[:, ti % 2, :]
                                 ).then_inc(out_stored, 16)
                    sp.wait_ge(out_stored, t * 16 + 16)
                    sp.sem_inc(result_stored, 1)
            for j in range(2):
                sp.wait_ge(x_in_ready[j], 16 * len(range(j, BATCH * TILES + PAD_TILES, 2)))

        @block.gpsimd
        def _(pool):
            pool.memset(ident[:, :], 0.0).then_inc(consts_made, 1)
            pool.memset(causal[:, :], 0.0).then_inc(mask_made, 1)
            pool.wait_ge(consts_made, 1)
            pool.affine_select(out=ident[:, :], in_=ident[:, :], compare_op=ALU.not_equal, fill=1.0, base=0,
                               pattern=[[-1, P]], channel_multiplier=1).then_inc(consts_made, 1)
            pool.wait_ge(mask_made, 1)
            pool.affine_select(out=causal[:, :], in_=causal[:, :], compare_op=ALU.is_ge, fill=MASKED, base=0,
                               pattern=[[-1, P]], channel_multiplier=1).then_inc(mask_made, 1)
            pool.memset(gnn_out[:, BATCH * TILES * P:], 0.0).then_inc(memsets_made, 1)
            with pool.Fori(0, BATCH * TILES) as t:
                for h in range(HEADS):
                    s = t * HEADS + h
                    pool.wait_ge(index_ready, s + 1)
                    pool.sem_inc(pool_gate, 1)
                    pool.wait_ge(combined, s + 1)
                    pool.sem_inc(pool_gate, 1)
                    for k in range(TOPK):
                        pool.indirect_dma_start(
                            out=rows[:, h % RING, k, :], out_offset=None, in_=table,
                            in_offset=bass.IndirectOffsetOnAxis(ap=row_index[:, h, k:k + 1], axis=0)
                        ).then_inc(rows_in[h], 16)

        @block.scalar
        def _(act):

            def make_fold():
                act.dma_start(wqpk_sb, wqpk_t).then_inc(fold_in, 16)
                act.dma_start(keys_sb[:, :], keys_t).then_inc(fold_in, 16)

            def evacuate_fold():
                act.wait_ge(fold_mm, 1)
                for i in range(4):
                    last = nc.scalar.activation(
                        fold[:, 2 * i:2 * i + 2, :, :].rearrange("p h s k -> p (h s k)"), bank[4 + i][:, :], ACT.Copy)
                last.then_inc(fold_made, 1)

            def prepare_adjacency():
                act.wait_ge(degree_made, 1)
                act.activation(root[:, :], degree[:, :], ACT.Sqrt).then_inc(degree_root, 1)
                act.wait_ge(dinv_made, 1)
                for m in range(TILES):
                    act.activation(adj_sb[:, m, :], adj_sb[:, m, :], ACT.Copy,
                                   scale=dinv[:, m:m + 1]).then_inc(adj_scaled, 1)
                ln_root(0, 0)
                for m in range(TILES):
                    act.wait_ge(adj_turned, m + 1)
                    act.activation(adj_t[:, m, :], bank[m][:, :], ACT.Copy,
                                   scale=dinv[:, m:m + 1]).then_inc(adj_t_made, 1)

            def ln_root(n, j):
                act.wait_ge(ln_stats, n + 1)
                act.activation(x_std[:, j, :], x_mv[:, j, :, 1], ACT.Sqrt, bias=eps[:, :]).then_inc(ln_std, 1)

            def first_layer(b2_, last):
                for j in range(2):
                    n = b2_ * 2 + j
                    act.wait_ge(agg_mm, n + 3)
                    act.activation(agg[:, j, :], bank[j][:, :], ACT.Copy).then_inc(agg_made, 1)
                    if not last:
                        ln_root(n + 2, j)
                    act.wait_ge(h1_mm, n + 1)
                    for c in range(CHUNKS):
                        last_one = act.activation(h1[:, c, bass.ds(n * SEQ, SEQ)], bank[2 + c][:, :], ACT.Identity,
                                                  bias=b1[:, c:c + 1])
                    last_one.then_inc(h1_made, 1)

            def second_layer():
                act.wait_ge(bn1_var, 1)
                act.activation(h_std[:, :], h_mv[:, :, 1], ACT.Sqrt, bias=eps[:, :]).then_inc(bn1_std, 1)
                act.wait_ge(bn1_made, 1)
                with act.Fori(0, BATCH // 2) as b2_:
                    for j in range(2):
                        n = b2_ * 2 + j
                        act.wait_ge(out_mm, n + 1)
                        for c in range(CHUNKS):
                            last_one = act.activation(hid_relu[:, j, c, :], h1[:, c, bass.ds(n * SEQ, SEQ)], ACT.Relu,
                                                      bias=h_shift[:, c:c + 1], scale=h_scale[:, c:c + 1])
                        last_one.then_inc(relu_made, 1)
                act.wait_ge(bn2_var, 1)
                act.activation(o_std[:, :], o_mv[:, :, 1], ACT.Sqrt, bias=eps[:, :]).then_inc(bn2_std, 1)

            def front_y(i):
                act.activation(y_t[:, :], gnn_out[:, bass.ds(i * P, P)], ACT.Identity,
                               bias=o_shift[:, :], scale=o_scale[:, :]).then_inc(y_made, 1)

            def front_root(i):
                act.wait_ge(x1_stats, i + 1)
                act.activation(t_std[:, :], t_mv[:, 1:2], ACT.Sqrt, bias=eps[:, :]).then_inc(x1_std, 1)

            def front_x2_t(i, j):
                act.wait_ge(x2_turned, i + 1)
                act.activation(x2_t[:, j, :], ps_turn[:, 0:P], ACT.Copy).then_inc(front_done, 1)

            def copy_scores(u, j):
                act.wait_ge(scores_mm, u + 1)
                act.activation(scores[:, j, :, :].rearrange("p s k -> p (s k)"), ps_scores[:, 0:2 * NUM_KEYS],
                               ACT.Copy).then_inc(scores_ready, 1)

            def candidate_exp(u):
                act.wait_ge(best_ready, u + 1)
                act.activation(sum_exp[:, :], cand[:, 0, :], ACT.Exp, bias=neg_best[:, :]).then_inc(exp_ready, 1)

            def make_diags(h, j, first, last):
                for k in range(first, last):
                    one = act.activation(diags[:, j, k, :], ident[:, :], ACT.Copy,
                                         scale=weight[:, h, DVE_ROWS + k:DVE_ROWS + k + 1])
                if last == PE_ROWS:
                    one.then_inc(diags_ready, 1)

            make_fold()
            evacuate_fold()
            act.wait_ge(memsets_made, 3)
            prepare_adjacency()
            ln_root(1, 1)
            act.wait_ge(small_in, 48)
            with act.Fori(0, BATCH // 2 - 1) as b2_:
                first_layer(b2_, last=False)
            first_layer(BATCH // 2 - 1, last=True)
            second_layer()

            act.wait_ge(bn2_made, 1)
            front_y(0)
            front_root(0)
            front_x2_t(0, 0)
            copy_scores(0, 0)
            copy_scores(1, 1)
            for u in range(PREP_AHEAD):
                candidate_exp(u)
                if u + 2 < SCORES_AHEAD:
                    act.wait_ge(weights_ready, u + 1)
                    copy_scores(u + 2, u % 2)
            make_diags(0, 0, 0, PE_ROWS)

            with act.Fori(0, BATCH) as b:
                for c in range(UNITS + 1):
                    s = b * UNITS + c
                    ti, h, j = c // HEADS, c % HEADS, c % 2
                    hn, jn = (c + 1) % HEADS, (c + 1) % 2
                    if c < UNITS:
                        act.wait_ge(weights_ready, s + 2)
                        act.wait_ge(combined, s + RING)
                        make_diags(hn, jn, 0, 2)
                    if c > 0:
                        keys = ((c - 1) // HEADS + 1) * P
                        act.wait_ge(max_ready, s)
                        act.activation(probs[:, 0:keys], ps_sim[:, 0:keys], ACT.Exp, bias=neg_max[:, jn:jn + 1],
                                       accum_out=prob_sum[:, jn:jn + 1]).then_inc(probs_exp, 1)
                    if c < UNITS:
                        make_diags(hn, jn, 2, 5)
                        if h == 0:
                            front_y(b * TILES + ti + 1)
                        if h == 1:
                            front_root(b * TILES + ti + 1)
                        if h == 2:
                            front_x2_t(b * TILES + ti + 1, (ti + 1) % 2)
                    if c > 0:
                        act.wait_ge(probs_turned, s)
                        act.activation(probs_t[:, 0:keys], ps_probs_t[:, 0:keys], ACT.Copy).then_inc(probs_t_ready, 1)
                    if c < UNITS:
                        candidate_exp(s + PREP_AHEAD)
                        make_diags(hn, jn, 5, PE_ROWS)
                        act.wait_ge(combined, s + RING + 1)
                        act.activation(k_now[:, :], ps_kv[:, 0:P], ACT.Copy, scale=weight_rsum[:, h:h + 1])
                        act.activation(v_store[:, h, ti, :], ps_kv[:, P:2 * P], ACT.Copy,
                                       scale=weight_rsum[:, h:h + 1]).then_inc(kv_ready, 1)
                    if c > 0:
                        act.wait_ge(att_mm, s)
                        act.activation(att_t[:, :], ps_att[:, 0:P], ACT.Copy).then_inc(att_ready, 1)
                    if c < UNITS:
                        copy_scores(s + SCORES_AHEAD, (c + SCORES_AHEAD) % 2)
                        act.wait_ge(kq_mm, s + 1)
                        act.activation(k_store[:, h, ti * P:(ti + 1) * P], ps_turn[:, 0:P], ACT.Copy)
                        act.activation(q_t[:, j, :], ps_turn[:, P:2 * P], ACT.Copy,
                                       scale=float(P) ** -0.5).then_inc(kq_ready, 1)

        @block.tensor
        def _(pe):
            mm = nc.tensor.matmul

            def make_fold():
                pe.wait_ge(fold_in, 32)
                for i in range(2 * HEADS):
                    cols = slice(i * P, (i + 1) * P)
                    last = mm(bank[4 + i // 4][:, (i % 4) * P:(i % 4 + 1) * P], wqpk_sb[:, cols], keys_sb[:, cols],
                              start=True, stop=True)
                last.then_inc(fold_mm, 1)

            def prepare_adjacency():
                pe.wait_ge(adj_plus_i, 1)
                for n in range(TILES):
                    for m in range(TILES):
                        last = mm(bank[0][:, n:n + 1], adj_sb[:, m, n * P:(n + 1) * P], ones[:, :],
                                  start=(m == 0), stop=(m == TILES - 1))
                last.then_inc(col_sums, 1)
                pe.wait_ge(adj_scaled, TILES)
                for m in range(TILES):
                    for n in range(TILES):
                        last = nc.tensor.transpose(bank[m][:, n * P:(n + 1) * P], adj_sb[:, n, m * P:(m + 1) * P],
                                                   ident[:, :])
                    last.then_inc(adj_turned, 1)

            def first_layer():
                pe.wait_ge(adj_t_made, TILES)
                pe.wait_ge(small_in, 48)
                pe.wait_ge(fold_made, 1)

                def aggregate(n, j):
                    pe.wait_ge(x_norm_made, n + 3)
                    for m in range(TILES):
                        one = mm(bank[j][:, :], x_norm[:, j, m * P:(m + 1) * P], adj_t[:, m, :],
                                 start=(m == 0), stop=(m == TILES - 1))
                    one.then_inc(agg_mm, 1)

                def two_elements(b2_, last):
                    for j in range(2):
                        n = b2_ * 2 + j
                        if not (last and j):
                            aggregate(n + 1, (j + 1) % 2)
                        pe.wait_ge(agg_made, n + 1)
                        for c in range(CHUNKS):
                            one = mm(bank[2 + c][:, :], w1_sb[:, c * P:(c + 1) * P], agg[:, j, :],
                                     start=True, stop=True)
                        one.then_inc(h1_mm, 1)

                aggregate(0, 0)
                with pe.Fori(0, BATCH // 2 - 1) as b2_:
                    two_elements(b2_, last=False)
                two_elements(BATCH // 2 - 1, last=True)

            def second_layer():
                with pe.Fori(0, BATCH // 2) as b2_:
                    for j in range(2):
                        n = b2_ * 2 + j
                        pe.wait_ge(relu_made, n + 1)
                        pe.wait_ge(gnn_out_made, n + 1)
                        for c in range(CHUNKS):
                            last = mm(bank[4 + j][:, :], w2_sb[:, c, :], hid_relu[:, j, c, :],
                                      start=(c == 0), stop=(c == CHUNKS - 1))
                        last.then_inc(out_mm, 1)

            def front_turn_y(i):
                pe.wait_ge(y_made, i + 1)
                nc.tensor.transpose(ps_turn[:, 0:P], y_t[:, :], ident[:, :]).then_inc(y_turned, 1)

            def front_turn_x2(i):
                pe.wait_ge(x2_made, i + 1)
                nc.tensor.transpose(ps_turn[:, 0:P], x2[:, :], ident[:, :]).then_inc(x2_turned, 1)

            def score(u, h, j):
                mm(ps_scores[:, 0:2 * NUM_KEYS], x2_t[:, j, :],
                   fold[:, h, :, :].rearrange("p s k -> p (s k)"), start=True, stop=True).then_inc(scores_mm, 1)

            make_fold()
            pe.wait_ge(memsets_made, 3)
            pe.wait_ge(consts_made, 2)
            prepare_adjacency()
            first_layer()
            second_layer()
            front_turn_y(0)
            front_turn_x2(0)
            pe.wait_ge(front_done, 1)
            for u in range(SCORES_AHEAD):
                if u > 0:
                    pe.wait_ge(scores_ready, u)
                score(u, u, 0)
            pe.wait_ge(attn_w_in, 32)

            def combine(c, first, last):
                for k in range(first, last):
                    mm(ps_kv[:, 0:2 * P], diags[:, c % 2, k, :], rows[:, (c % HEADS) % RING, DVE_ROWS + k, :],
                       start=(k == 0), stop=False)

            with pe.Fori(0, BATCH) as b:
                for c in range(UNITS + 1):
                    s = b * UNITS + c
                    ti, h, j = c // HEADS, c % HEADS, c % 2
                    tp, hp, jp = (c - 1) // HEADS, (c - 1) % HEADS, (c - 1) % 2
                    if c < UNITS:
                        pe.wait_ge(diags_ready, s + 1)
                        pe.wait_ge(rows_in[h], (b * TILES + ti + 1) * (16 * TOPK))
                        combine(c, 0, 3)
                    if c > 0:
                        pe.wait_ge(kq_ready, s)
                        mm(ps_sim[:, 0:(tp + 1) * P], q_t[:, jp, :], k_store[:, hp, 0:(tp + 1) * P],
                           start=True, stop=True).then_inc(sim_ready, 1)
                    if c < UNITS:
                        if h == 1:
                            front_turn_y(b * TILES + ti + 1)
                        if h == 2:
                            front_turn_x2(b * TILES + ti + 1)
                        combine(c, 3, PE_ROWS)
                    if c > 0:
                        pe.wait_ge(probs_ready, s)
                        for m in range(tp + 1):
                            last = nc.tensor.transpose(ps_probs_t[:, m * P:(m + 1) * P], probs[:, m * P:(m + 1) * P],
                                                       ident[:, :])
                        last.then_inc(probs_turned, 1)
                    if c < UNITS:
                        pe.wait_ge(part_ready, s + 1)
                        mm(ps_kv[:, 0:2 * P], ident[:, :], kv_part[:, :], start=False, stop=True).then_inc(combined, 1)
                    if c > 0:
                        pe.wait_ge(probs_t_ready, s)
                        for m in range(tp + 1):
                            last = mm(ps_att[:, 0:P], v_store[:, hp, m, :], probs_t[:, m * P:(m + 1) * P],
                                      start=(m == 0), stop=(m == tp))
                        last.then_inc(att_mm, 1)
                    if c < UNITS:
                        pe.wait_ge(scores_ready, s + SCORES_AHEAD)
                        cs = c + SCORES_AHEAD
                        if cs % HEADS == 0:
                            pe.wait_ge(front_done, b * TILES + cs // HEADS + 1)
                        score(s + SCORES_AHEAD, cs % HEADS, (cs // HEADS) % 2)
                        pe.wait_ge(kv_ready, s + 1)
                        if h == 1:
                            pe.wait_ge(x1_stats, b * TILES + ti + 2)
                        if h == 2:
                            pe.wait_ge(front_done, b * TILES + ti + 2)
                        nc.tensor.transpose(ps_turn[:, 0:P], k_now[:, :], ident[:, :])
                        mm(ps_turn[:, P:2 * P], wq_sb[:, h * P:(h + 1) * P], x2_t[:, ti % 2, :],
                           start=True, stop=True).then_inc(kq_mm, 1)
                    if c > 0:
                        pe.wait_ge(att_ready, s)
                        if hp == 0:
                            pe.wait_ge(result_ready, b * TILES + tp + 1)
                        last = mm(ps_y[:, 0:P], att_t[:, :], wo_sb[:, hp, :], start=(hp == 0), stop=(hp == HEADS - 1))
                        if hp == HEADS - 1:
                            last.then_inc(y_done, 1)

        @block.vector
        def _(dve):
            v = nc.vector
            own = Chain(dve, dve_own)

            def degrees():
                dve.wait_ge(adj_in, 16)
                dve.wait_ge(consts_made, 2)
                for m in range(TILES):
                    part = adj_sb[:, m, m * P:(m + 1) * P]
                    own.add(v.tensor_tensor(out=part, in0=part, in1=ident[:, :], op=ALU.add))
                own.wait()
                v.reduce_sum(row_sum[:, :], adj_sb, axis=AX.X).then_inc(adj_plus_i, 1)
                for m in range(TILES):
                    own.add(v.tensor_tensor(out=diag_tmp[:, m, :], in0=adj_sb[:, m, m * P:(m + 1) * P],
                                            in1=ident[:, :], op=ALU.mult))
                own.wait()
                own.add(v.reduce_sum(diag_sum[:, :], diag_tmp, axis=AX.X))
                own.wait()
                own.add(v.tensor_tensor(out=row_sum[:, :], in0=row_sum[:, :], in1=diag_sum[:, :], op=ALU.subtract))
                own.wait()
                dve.wait_ge(col_sums, 1)
                v.tensor_tensor(out=degree[:, :], in0=bank[0][:, 0:TILES], in1=row_sum[:, :],
                                op=ALU.add).then_inc(degree_made, 1)
                dve.wait_ge(degree_root, 1)
                v.reciprocal(dinv[:, :], root[:, :]).then_inc(dinv_made, 1)

            def layer_norm(n, b2_, j):
                dve.wait_ge(x_batch_in[j], b2_ * 16 + 16)
                for m in range(TILES):
                    own.add(v.bn_stats(x_stats[:, m, :], x_batch[:, j, m * P:(m + 1) * P]))
                own.wait()
                for m in range(TILES):
                    last = v.bn_aggr(x_mv[:, j, m, :], x_stats[:, m, :])
                last.then_inc(ln_stats, 1)
                dve.wait_ge(ln_std, n + 1)
                own.add(v.reciprocal(x_rstd[:, :], x_std[:, j, :]))
                own.wait()
                dve.wait_ge(agg_mm, n + 1)
                for m in range(TILES):
                    last = v.tensor_scalar(x_norm[:, j, m * P:(m + 1) * P], x_batch[:, j, m * P:(m + 1) * P],
                                           x_mv[:, j, m, 0:1], x_rstd[:, m:m + 1], ALU.subtract, ALU.mult)
                last.then_inc(x_norm_made, 1)

            def first_layer(b2_, last):
                for j in range(2):
                    n = b2_ * 2 + j
                    if not last:
                        layer_norm(n + 2, b2_ + 1, j)
                    dve.wait_ge(h1_made, n + 1)
                    for c in range(CHUNKS):
                        own.add(v.bn_stats(h_stats[:, c, bass.ds(n * 6, 6)], h1[:, c, bass.ds(n * SEQ, SEQ)]))
                own.restart()

            def batch_norm(mv, stats, std, scale, tmp, shift, gamma, beta, var_ready, std_ready, made):
                own.wait()
                for c in range(mv.shape[1]):
                    last = v.bn_aggr(mv[:, c, :], stats[c])
                last.then_inc(var_ready, 1)
                dve.wait_ge(std_ready, 1)
                own.add(v.reciprocal(scale, std))
                own.wait()
                own.add(v.tensor_tensor(out=scale, in0=scale, in1=gamma, op=ALU.mult))
                own.wait()
                own.add(v.tensor_tensor(out=tmp, in0=mv[:, :, 0], in1=scale, op=ALU.mult))
                own.wait()
                v.tensor_tensor(out=shift, in0=beta, in1=tmp, op=ALU.subtract).then_inc(made, 1)

            def front_x1(i, j, halves):
                dve.wait_ge(y_turned, i + 1)
                dve.wait_ge(x_in_ready[j], halves * 16 + 16)
                own.add(v.tensor_tensor(out=x1[:, j, :], in0=ps_turn[:, 0:P], in1=x_in[:, j, :], op=ALU.add))
                own.wait()
                own.add(v.bn_stats(t_stats[:, :], x1[:, j, :]))
                own.wait()
                v.bn_aggr(t_mv[:, :], t_stats[:, :]).then_inc(x1_stats, 1)

            def front_x2(i, j):
                dve.wait_ge(x1_std, i + 1)
                own.add(v.reciprocal(t_rstd[:, :], t_std[:, :]))
                own.wait()
                v.tensor_scalar(x2[:, :], x1[:, j, :], t_mv[:, 0:1], t_rstd[:, :],
                                ALU.subtract, ALU.mult).then_inc(x2_made, 1)

            def pick_halves(u, j):
                dve.wait_ge(scores_ready, u + 1)
                dve.sem_inc(dve_gate, 1)
                sc = scores[:, j, :, :]
                for p in range(2):
                    own.add(v.max(top[:, 0, p, 0:8], sc[:, p, :]))
                own.wait()
                for p in range(2):
                    own.add(v.match_replace(rest[:, p, :], top[:, 0, p, 0:8], sc[:, p, :], LOWEST))
                for p in range(2):
                    own.add(v.max_index(top_i[:, p, 0:8], top[:, 0, p, 0:8], sc[:, p, :]))
                own.wait()
                for p in range(2):
                    own.add(v.max(top[:, 0, p, 8:16], rest[:, p, :]))
                own.wait()
                for p in range(2):
                    own.add(v.max_index(top_i[:, p, 8:16], top[:, 0, p, 8:16], rest[:, p, :]))
                own.wait()
                unit = float(1 << ROW_SHIFT)
                own.add(v.tensor_scalar(top[:, 1, 0, :], top_i[:, 0, :], unit, None, ALU.mult))
                own.add(v.tensor_scalar(top[:, 1, 1, :], top_i[:, 1, :], unit * NUM_KEYS, unit * ROW_BIAS,
                                        ALU.mult, ALU.add))
                own.wait()

            def pick_sums(u):
                at = 0
                for i0, n, m in BLOCKS:
                    shape = [P, 2, n, m]
                    own.add(v.tensor_tensor(
                        out=cand[:, :, at:at + n * m].rearrange("p q (i j) -> p q i j", i=n),
                        in0=top[:, :, 0, i0:i0 + n].unsqueeze(3).to_broadcast(shape),
                        in1=top[:, :, 1, 0:m].unsqueeze(2).to_broadcast(shape), op=ALU.add))
                    at += n * m
                own.wait()
                own.add(v.max(best[:, 0:8], cand[:, 0, :]))
                own.wait()
                v.tensor_scalar(neg_best[:, :], best[:, 0:1], -1.0, None, ALU.mult).then_inc(best_ready, 1)
                own.add(v.match_replace(left1[:, :], best[:, 0:8], cand[:, 0, :], LOWEST))
                own.wait()
                own.add(v.max(best[:, 8:16], left1[:, :]))
                own.wait()
                own.add(v.match_replace(left2[:, :], best[:, 8:16], left1[:, :], LOWEST))
                own.wait()
                own.add(v.scalar_tensor_tensor(out=picked[:, :], in0=left2[:, :], scalar=LOWEST, in1=cand[:, 1, :],
                                               op0=ALU.is_equal, op1=ALU.mult))

            def pack_and_sort(u, h):
                own.wait()
                dve.wait_ge(exp_ready, u + 1)
                bits = sum_exp[:, :].bitcast(i32)
                own.add(v.scalar_tensor_tensor(out=code[:, 0, :], in0=bits, scalar=LOW_BITS, in1=picked[:, :],
                                               op0=ALU.logical_shift_right, op1=ALU.bitwise_or))
                own.add(v.scalar_tensor_tensor(out=code[:, 1, :], in0=bits, scalar=(1 << LOW_BITS) - 1,
                                               in1=picked[:, :], op0=ALU.bitwise_and, op1=ALU.bitwise_or))
                own.wait()
                for p in range(2):
                    own.add(v.max(got[:, p, 0:8], code[:, p, :].bitcast(f32)))
                own.wait()
                for p in range(2):
                    own.add(v.match_replace(code_left[:, p, :], got[:, p, 0:8], code[:, p, :].bitcast(f32), 0.0))
                own.wait()
                for p in range(2):
                    own.add(v.max(got[:, p, 8:16], code_left[:, p, :]))
                own.wait()
                own.add(v.tensor_scalar(got_row[:, :], got[:, 0, :].bitcast(i32), ROW_SHIFT, None,
                                        ALU.logical_shift_right))
                own.add(v.tensor_scalar(got_high[:, :], got[:, 0, :].bitcast(i32), (1 << ROW_SHIFT) - 1, LOW_BITS,
                                        ALU.bitwise_and, ALU.logical_shift_left))
                own.wait()
                v.tensor_scalar(row_index[:, h, :], got_row[:, :], float(h * NUM_KV - ROW_BIAS), None,
                                ALU.add).then_inc(index_ready, 1)
                own.add(v.scalar_tensor_tensor(out=weight[:, h, :].bitcast(i32), in0=got[:, 1, :].bitcast(i32),
                                               scalar=(1 << LOW_BITS) - 1, in1=got_high[:, :],
                                               op0=ALU.bitwise_and, op1=ALU.bitwise_or))
                own.wait()
                own.add(v.reduce_sum(weight_sum[:, :], weight[:, h, :], axis=AX.X))
                own.wait()
                v.reciprocal(weight_rsum[:, h:h + 1], weight_sum[:, :]).then_inc(weights_ready, 1)

            def combine_part(h):
                r = h % RING
                own.add(v.tensor_scalar(ps_part[:, 0:2 * P], rows[:, r, 0, :], weight[:, h, 0:1], None, ALU.mult))
                for k in range(1, DVE_ROWS - 1):
                    own.wait()
                    own.add(v.scalar_tensor_tensor(out=ps_part[:, 0:2 * P], in0=rows[:, r, k, :],
                                                   scalar=weight[:, h, k:k + 1], in1=ps_part[:, 0:2 * P],
                                                   op0=ALU.mult, op1=ALU.add))
                own.wait()
                k = DVE_ROWS - 1
                v.scalar_tensor_tensor(out=kv_part[:, :], in0=rows[:, r, k, :], scalar=weight[:, h, k:k + 1],
                                       in1=ps_part[:, 0:2 * P], op0=ALU.mult, op1=ALU.add).then_inc(part_ready, 1)

            v.memset(eps[:, :], EPS).then_inc(memsets_made, 1)
            v.memset(ones[:, :], 1.0).then_inc(memsets_made, 1)
            dve.sem_inc(x_norm_made, 2)
            dve.sem_inc(agg_mm, 2)
            dve.sem_inc(out_mm, 2)
            dve.sem_inc(gnn_out_made, 2)
            dve.sem_inc(combined, RING)
            dve.sem_inc(result_ready, 1)
            dve.sem_inc(result_stored, 2)
            degrees()
            own.restart()
            layer_norm(0, 0, 0)
            layer_norm(1, 0, 1)
            own.restart()
            with dve.Fori(0, BATCH // 2 - 1) as b2_:
                first_layer(b2_, last=False)
            first_layer(BATCH // 2 - 1, last=True)
            dve.wait_ge(small_in, 48)
            batch_norm(h_mv, [h_stats[:, c, :] for c in range(CHUNKS)], h_std[:, :], h_scale[:, :], h_tmp[:, :],
                       h_shift[:, :], g1, be1, bn1_var, bn1_std, bn1_made)
            own.restart()
            with dve.Fori(0, BATCH // 2) as b2_:
                for j in range(2):
                    n = b2_ * 2 + j
                    dve.wait_ge(out_mm, n + 3)
                    v.tensor_scalar(gnn_out[:, bass.ds(n * SEQ, SEQ)], bank[4 + j][:, :], b2, None,
                                    ALU.add).then_inc(gnn_out_made, 1)
                    dve.wait_ge(gnn_out_made, n + 3)
                    own.add(v.bn_stats(o_stats[:, bass.ds(n * 6, 6)], gnn_out[:, bass.ds(n * SEQ, SEQ)]))
                own.restart()
            batch_norm(o_mv, [o_stats[:, :]], o_std[:, :], o_scale[:, :], o_tmp[:, :],
                       o_shift[:, :], g2, be2, bn2_var, bn2_std, bn2_made)
            own.restart()
            front_x1(0, 0, 0)
            front_x2(0, 0)
            for u in range(PREP_AHEAD):
                pick_halves(u, u % 2)
                pick_sums(u)
                pack_and_sort(u, u)
            dve.wait_ge(mask_made, 2)
            own.restart()

            with dve.Fori(0, BATCH) as b:
                for c in range(UNITS + 1):
                    s = b * UNITS + c
                    ti, h, j = c // HEADS, c % HEADS, c % 2
                    tp, hp, jp = (c - 1) // HEADS, (c - 1) % HEADS, (c - 1) % 2

                    def finish_tile(tile, half):
                        dve.wait_ge(y_done, b * TILES + tile + 1)
                        dve.wait_ge(result_stored, b * TILES + tile + 1)
                        v.tensor_tensor(out=result[:, half, :], in0=ps_y[:, 0:P], in1=x1[:, half, :],
                                        op=ALU.add).then_inc(result_ready, 1)
                        dve.wait_ge(result_ready, b * TILES + tile + 2)

                    def finish_softmax(half, tile):
                        dve.wait_ge(probs_exp, s)
                        own.add(v.reciprocal(prob_rsum[:, :], prob_sum[:, half:half + 1]))
                        own.wait()
                        v.tensor_scalar(probs[:, 0:(tile + 1) * P], probs[:, 0:(tile + 1) * P], prob_rsum[:, :], None,
                                        ALU.mult).then_inc(probs_ready, 1)

                    if c > 0:
                        dve.wait_ge(sim_ready, s)
                        own.add(v.tensor_tensor(out=ps_sim[:, tp * P:(tp + 1) * P], in0=ps_sim[:, tp * P:(tp + 1) * P],
                                                in1=causal[:, :], op=ALU.add))
                        own.wait()
                        v.tensor_reduce(neg_max[:, jp:jp + 1], ps_sim[:, 0:(tp + 1) * P], AX.X, ALU.max,
                                        negate=True).then_inc(max_ready, 1)
                    if c < UNITS:
                        if h == 1:
                            if c > HEADS:
                                finish_tile(ti - 1, (ti - 1) % 2)
                            front_x1(b * TILES + ti + 1, (ti + 1) % 2, b * 2 + (ti + 1) // 2)
                        if h == 2:
                            front_x2(b * TILES + ti + 1, (ti + 1) % 2)
                        dve.wait_ge(rows_in[h], (b * TILES + ti + 1) * (16 * TOPK))
                        combine_part(h)
                    if c > 0:
                        finish_softmax(jp, tp)
                    if c < UNITS:
                        pick_halves(s + PREP_AHEAD, (c + PREP_AHEAD) % 2)
                        pick_sums(s + PREP_AHEAD)
                        pack_and_sort(s + PREP_AHEAD, (c + PREP_AHEAD) % HEADS)
                    else:
                        finish_tile(TILES - 1, (TILES - 1) % 2)
                        dve.sem_inc(dve_gate, 1)
                own.restart()


def kernel(x, adj, L0_gnn_W1, L0_gnn_b1, L0_gnn_g1, L0_gnn_be1, L0_gnn_W2, L0_gnn_b2, L0_gnn_g2, L0_gnn_be2,
           L0_ffn_Wq_pk, L0_ffn_pk_keys, L0_ffn_Wq, L0_ffn_keys_table, L0_ffn_values_table, L0_ffn_Wo):
    import numpy as np
    import concourse.bacc as bacc
    from concourse.bass_utils import run_bass_kernel_spmd

    def lay(a):
        return np.ascontiguousarray(a)

    def columns(a):
        return np.asarray(a).reshape(-1, P).T

    x = np.asarray(x)
    half = (2, HEADS, DIM_KEY)
    arrays = {
        "x": lay(np.concatenate([x.reshape(-1, P), np.zeros((PAD_TILES * P, P), x.dtype)], axis=0)),
        "adj": lay(adj),
        "vecs": lay(np.concatenate([columns(a) for a in (L0_gnn_b1, L0_gnn_g1, L0_gnn_be1, L0_gnn_b2, L0_gnn_g2,
                                                         L0_gnn_be2)], axis=1)),
        "w1t": lay(np.asarray(L0_gnn_W1).T),
        "w2t": lay(np.asarray(L0_gnn_W2).T.reshape(CHUNKS, P, P).transpose(1, 0, 2)),
        "wqpk_t": lay(np.asarray(L0_ffn_Wq_pk).reshape(P, *half).transpose(3, 2, 1, 0).reshape(DIM_KEY, -1)),
        "keys_t": lay(np.asarray(L0_ffn_pk_keys).transpose(3, 2, 0, 1).reshape(DIM_KEY, -1)),
        "wq": lay(L0_ffn_Wq),
        "table": lay(np.concatenate([L0_ffn_keys_table, L0_ffn_values_table], axis=1)),
        "wo": lay(np.asarray(L0_ffn_Wo).reshape(HEADS, P, P).transpose(1, 0, 2)),
    }
    nc = bacc.Bacc("TRN2", target_bir_lowering=False, num_devices=1)
    aps = [nc.dram_tensor(n, a.shape, mybir.dt.from_np(a.dtype), kind="ExternalInput").ap() for n, a in arrays.items()]
    out = nc.dram_tensor("out", (BATCH, SEQ, P), mybir.dt.float32, kind="ExternalOutput").ap()
    build(nc, *aps, out)
    return run_bass_kernel_spmd(nc, [arrays], core_ids=[0]).results[0]["out"]
```
